# Optimizing a Trainium2 kernel written in Bass

```python
import numpy as np
import jax
import jax.numpy as jnp

def _softmax(x, axis=-1):
    return jax.nn.softmax(x, axis=axis)

def _gelu(x):
    return jax.nn.gelu(x, approximate=True)

def _silu(x):
    return jax.nn.silu(x)

def _sigmoid(x):
    return jax.nn.sigmoid(x)

def _layernorm(x, axis=-1, eps=1e-05):
    m = jnp.mean(x, axis=axis, keepdims=True)
    v = jnp.var(x, axis=axis, keepdims=True)
    return (x - m) / jnp.sqrt(v + eps)

def _scatter_add(tgt, idx, src, axis=0):
    return tgt.at[idx].add(src)

def _segment_sum(src, seg, n):
    return jax.ops.segment_sum(src, seg, n)
kernel_name = 'mk_rec_standalone_d1_rec_r8_c40a51'

def setup_inputs(seed: int=0):
    np.random.seed(seed)
    _w = jnp.asarray

    def _rec_inputs():
        import jax
        import jax.numpy as jnp
        _rk = jax.random.key(seed)
        r_wfts = jax.random.uniform(jax.random.fold_in(_rk, 1), (1024, 5120), jnp.float32, 0.0, 1)
        r_bfts = jax.random.uniform(jax.random.fold_in(_rk, 2), (1024, 5120), jnp.float32, 0.0, 1)
        r_stm = jax.random.uniform(jax.random.fold_in(_rk, 3), (1024, 1), jnp.float32, 0.0, 0.999707)
        return (r_wfts, r_bfts, r_stm)
    r_wfts, r_bfts, r_stm = _rec_inputs()

    def _L0_rec_setup():
        import jax, jax.numpy as jnp
        import numpy as np
        NUM_FEATURES = 5120
        key = jax.random.key(seed)
        ks = jax.random.split(key, 9)
        B = 512
        wfts = jax.random.uniform(ks[0], (B, NUM_FEATURES), dtype=jnp.float32)
        bfts = jax.random.uniform(ks[1], (B, NUM_FEATURES), dtype=jnp.float32)
        stm = jax.random.uniform(ks[2], (B, 1), dtype=jnp.float32)
        s_ft = 1.0 / np.sqrt(NUM_FEATURES)
        ft_w = jax.random.uniform(ks[3], (4, NUM_FEATURES), jnp.float32, -s_ft, s_ft)
        ft_b = jax.random.uniform(ks[4], (4,), jnp.float32, -s_ft, s_ft)
        s1 = 1.0 / np.sqrt(8.0)
        l1_w = jax.random.uniform(ks[5], (8, 8), jnp.float32, -s1, s1)
        l1_b = jax.random.uniform(ks[6], (8,), jnp.float32, -s1, s1)
        l2_w = jax.random.uniform(ks[7], (1, 8), jnp.float32, -s1, s1)
        l2_b = jax.random.uniform(ks[8], (1,), jnp.float32, -s1, s1)
        return {'wfts': wfts, 'bfts': bfts, 'stm': stm, 'ft_w': ft_w, 'ft_b': ft_b, 'l1_w': l1_w, 'l1_b': l1_b, 'l2_w': l2_w, 'l2_b': l2_b}
    _L0_rec_all = _L0_rec_setup()
    _L0_rec_in = {k: v for k, v in _L0_rec_all.items() if k in ('ft_w', 'ft_b', 'l1_w', 'l1_b', 'l2_w', 'l2_b')}
    del _L0_rec_all
    return {'r_wfts': r_wfts, 'r_bfts': r_bfts, 'r_stm': r_stm, 'L0_rec_ft_w': _L0_rec_in['ft_w'], 'L0_rec_ft_b': _L0_rec_in['ft_b'], 'L0_rec_l1_w': _L0_rec_in['l1_w'], 'L0_rec_l1_b': _L0_rec_in['l1_b'], 'L0_rec_l2_w': _L0_rec_in['l2_w'], 'L0_rec_l2_b': _L0_rec_in['l2_b']}

def reference(r_wfts, r_bfts, r_stm, L0_rec_ft_w, L0_rec_ft_b, L0_rec_l1_w, L0_rec_l1_b, L0_rec_l2_w, L0_rec_l2_b):
    import jax
    import jax.numpy as jnp

    def _L0_rec_ref(wfts, bfts, stm, ft_w, ft_b, l1_w, l1_b, l2_w, l2_b):
        import jax, jax.numpy as jnp
        import numpy as np
        NUM_FEATURES = 5120
        w = jnp.einsum('bf,of->bo', wfts, ft_w) + ft_b
        b = jnp.einsum('bf,of->bo', bfts, ft_w) + ft_b
        acc = stm * jnp.concatenate([w, b], axis=1) + (1.0 - stm) * jnp.concatenate([b, w], axis=1)
        l1_x = jnp.clip(acc, 0.0, 1.0)
        l2_x = jnp.clip(jnp.einsum('bi,oi->bo', l1_x, l1_w) + l1_b, 0.0, 1.0)
        return jnp.einsum('bi,oi->bo', l2_x, l2_w) + l2_b
    y = _L0_rec_ref(r_wfts, r_bfts, r_stm, L0_rec_ft_w, L0_rec_ft_b, L0_rec_l1_w, L0_rec_l1_b, L0_rec_l2_w, L0_rec_l2_b)
    return y

_drawn_inputs = setup_inputs


def setup_inputs(seed=0):
    import zlib

    import numpy as np

    out = dict(_drawn_inputs(seed))
    spreads = {}
    factors = {'r_stm': 3.029, 'L0_rec_ft_b': 59.301}
    for name, (base, spread) in spreads.items():
        noise = np.random.default_rng([zlib.crc32(name.encode()), seed]).standard_normal(out[name].shape)
        drawn = base * np.exp(spread * noise) if base else spread * noise
        out[name] = jnp.asarray(drawn.astype(out[name].dtype))
    for name, factor in factors.items():
        out[name] = (out[name] * factor).astype(out[name].dtype)
    return out
```

```python
from contextlib import ExitStack

import numpy as np

import concourse.bass as bass
from concourse import mybir
from concourse.alu_op_type import AluOpType as ALU

F32 = mybir.dt.float32

P = 128
Q = 32
NQ = P // Q
ROWS, FEATURES = 1024, 5120
TILES = ROWS // P
OUT1 = 4
HID = 2 * OUT1
N = TILES * Q

CHUNKS = 8
UNIT_F = FEATURES // CHUNKS
BLOCKS = UNIT_F // Q
HALF = BLOCKS // 2
SIDES = 2
STEP_CHUNKS = 2
STEP_UNITS = STEP_CHUNKS * SIDES
RAW_SLOTS = STEP_UNITS
T_SLOTS = 4
STEPS = CHUNKS // STEP_CHUNKS
UNITS = CHUNKS * SIDES
TAIL = [(0, 10), (10, 4), (14, 3), (17, 3)]

GROUPS = NQ
GN = N // GROUPS
PAIRS = GROUPS * NQ

C_SEL, C_MASK, C_OFF, C_REST, C_L2W, C_L2B, C_END = np.cumsum([0, Q, PAIRS, 1, 1, 1, 1]).tolist()
R_SIGN, R_EYE, R_L1W, R_STM, R_FTB, R_L1B, R_END = np.cumsum([0, P, HID, P, N, Q, P]).tolist()


def lay_out_parameters(stm, ft_b, l1_w, l1_b, l2_w, l2_b):
    p = np.arange(P)
    second = p % HID >= OUT1
    cols = np.zeros((P, C_END), np.float32)
    cols[p, C_SEL + p % Q] = 1
    cols[p, C_MASK + p // HID] = 1
    cols[:, C_OFF] = second
    cols[:, C_REST] = ~second
    cols[:, C_L2W] = np.tile(l2_w[0], PAIRS)
    cols[:, C_L2B] = l2_b[0]
    rows = np.zeros((HID, R_END), np.float32)
    rows[p % Q // HID, R_SIGN + p] = np.where(second, -1, 1)
    rows[np.arange(HID), R_EYE + np.arange(HID)] = 1
    rows[:, R_L1W:R_L1W + P] = np.tile(l1_w, (1, PAIRS))
    rows[:NQ, R_STM:R_STM + N] = stm.reshape(TILES, NQ, Q).transpose(1, 0, 2).reshape(NQ, N)
    rows[0, R_FTB:R_FTB + Q] = np.tile(ft_b, Q // OUT1)
    rows[0, R_L1B:R_L1B + P] = np.tile(l1_b, PAIRS)
    return cols, rows


def evaluate(nc, wfts, bfts, ft_w, param_cols, param_rows, out):
    feats = [x.rearrange("(t p) f -> p t f", p=P) for x in (wfts, bfts)]

    with ExitStack() as ctx:
        def sb(name, shape):
            return ctx.enter_context(nc.sbuf_tensor(name, shape, F32))

        def ps(name, shape):
            return ctx.enter_context(nc.psum_tensor(name, shape, F32))

        def sem(name):
            return ctx.enter_context(nc.semaphore(name))

        raw = [sb(f"raw{s}", [P, TILES, UNIT_F]) for s in range(RAW_SLOTS)]
        turned = [sb(f"turned{s}", [P, HALF, TILES, Q]) for s in range(T_SLOTS)]
        w_rows = sb("w_rows", [Q, BLOCKS, Q])
        w_cols = sb("w_cols", [Q, BLOCKS, CHUNKS, OUT1])
        w_diag = [sb(f"w_diag{s}", [P, BLOCKS, NQ, 2, OUT1]) for s in range(STEP_CHUNKS)]
        cols = sb("cols", [P, C_END])
        rows = sb("rows", [HID, R_END])
        zero_row = sb("zero_row", [1, Q])
        one_row = sb("one_row", [1, N])
        mix = [sb(f"mix{s}", [P, N]) for s in range(SIDES)]
        l1_diag = sb("l1_diag", [P, PAIRS, HID])
        l2_diag = sb("l2_diag", [P, PAIRS])
        mixed = [sb(f"mixed{s}", [P, N]) for s in range(SIDES)]
        x1 = sb("x1", [P, GN])
        x2 = sb("x2", [P, GN])
        y_out = sb("y_out", [PAIRS, GN])

        acc = [ps(f"acc{s}", [P, 512]) for s in range(SIDES)]
        p_stm = ps("p_stm", [P, 512])
        p_l1w = ps("p_l1w", [P, 512])
        p_x1 = ps("p_x1", [P, 512])
        p_x2 = ps("p_x2", [P, 512])
        p_y = ps("p_y", [P, 512])

        loaded = [sem(f"loaded{s}") for s in range(RAW_SLOTS)]
        tail_loaded = [sem(f"tail_loaded{i}") for i in range(len(TAIL))]
        w_in = sem("w_in")
        rows_in = sem("rows_in")
        cols_in = sem("cols_in")
        rows_set = sem("rows_set")
        diag_zeroed = sem("diag_zeroed")
        w_turned = sem("w_turned")
        w_ready = sem("w_ready")
        halves_turned = sem("halves_turned")
        t_free = sem("t_free")
        b_summed = sem("b_summed")
        stm_spread = sem("stm_spread")
        l1_turned = sem("l1_turned")
        mix_ready = sem("mix_ready")
        l1_ready = sem("l1_ready")
        l2_ready = sem("l2_ready")
        w_mixed = sem("w_mixed")
        b_mixed = sem("b_mixed")
        x1_sum = sem("x1_sum")
        x1_ready = sem("x1_ready")
        x2_sum = sem("x2_sum")
        x2_ready = sem("x2_ready")
        y_sum = sem("y_sum")
        y_ready = sem("y_ready")
        stored = sem("stored")

        block = ctx.enter_context(nc.Block())

        @block.sync
        def _(sp):
            def load(side, chunk, slot, first=0, blocks=BLOCKS):
                f = chunk * UNIT_F + first * Q
                return sp.dma_start(raw[slot][:, :, first * Q:(first + blocks) * Q],
                                    feats[side][:, :, bass.ds(f, blocks * Q)])

            for u in range(STEP_UNITS):
                load(u % SIDES, u // SIDES, u).then_inc(loaded[u], 16)
            with sp.Fori(1, STEPS - 1) as step:
                for u in range(STEP_UNITS):
                    sp.wait_ge(halves_turned, step * (2 * STEP_UNITS) + (2 * (u + 1) - 2 * STEP_UNITS))
                    load(u % SIDES, step * STEP_CHUNKS + u // SIDES, u).then_inc(loaded[u], 16)
            for u in range(STEP_UNITS):
                sp.wait_ge(halves_turned, 2 * ((STEPS - 2) * STEP_UNITS + u + 1))
                chunk = CHUNKS - STEP_CHUNKS + u // SIDES
                if u < STEP_UNITS - 1:
                    load(u % SIDES, chunk, u).then_inc(loaded[u], 16)
                else:
                    for i, (first, blocks) in enumerate(TAIL):
                        load(u % SIDES, chunk, u, first, blocks).then_inc(tail_loaded[i], 16)
            sp.wait_ge(y_ready, 1)
            sp.dma_start(out.rearrange("(a b r) o -> b a (r o)", a=TILES // GROUPS, r=Q),
                         y_out[:].rearrange("b (a r) -> b a r", r=Q)).then_inc(stored, 16)
            sp.wait_ge(stored, 16)

        @block.gpsimd
        def _(pool):
            nc.gpsimd.memset(zero_row[:], 0.0).then_inc(rows_set, 1)
            nc.gpsimd.memset(one_row[:], 1.0).then_inc(rows_set, 1)
            for s in range(STEP_CHUNKS):
                nc.gpsimd.memset(w_diag[s][:], 0.0).then_inc(diag_zeroed, 1)

        @block.scalar
        def _(act):
            act.dma_start(rows[:], param_rows).then_inc(rows_in, 16)
            act.dma_start(w_rows[:].rearrange("p b f -> p (b f)"),
                          ft_w.rearrange("o (c f) -> c o f", c=CHUNKS)).then_inc(w_in, 16)
            act.dma_start(cols[:], param_cols).then_inc(cols_in, 16)

            def lay_out(chunk, s):
                for q in range(NQ):
                    for twice in range(2):
                        last = nc.scalar.copy(w_diag[s][q * Q:(q + 1) * Q, :, q, twice, :],
                                              w_cols[:, :, bass.ds(chunk, 1), :].rearrange("p b a o -> p b (a o)"))
                    last.then_inc(w_ready, 1)

            act.wait_ge(diag_zeroed, STEP_CHUNKS)
            act.wait_ge(w_turned, 1)
            for s in range(STEP_CHUNKS):
                lay_out(s, s)
            with act.Fori(1, STEPS) as step:
                for s in range(STEP_CHUNKS):
                    act.wait_ge(t_free, step * (2 * STEP_UNITS) + (T_SLOTS + 2 * SIDES * (s + 1 - STEP_CHUNKS)))
                    lay_out(step * STEP_CHUNKS + s, s)

        @block.vector
        def _(dve):
            dve.wait_ge(w_in, 16)
            nc.vector.transpose(w_cols[:].rearrange("p b c o -> p (b c o)"),
                                w_rows[:].rearrange("p b f -> p (b f)")).then_inc(w_turned, 1)
            dve.wait_ge(cols_in, 16)
            dve.wait_ge(stm_spread, 1)
            nc.vector.tensor_scalar(mix[0][:], p_stm[:, 0:N], cols[:, C_OFF:C_OFF + 1], None,
                                    ALU.add).then_inc(mix_ready, 1)
            nc.vector.tensor_scalar(mix[1][:], p_stm[:, 0:N], -1.0, cols[:, C_REST:C_REST + 1],
                                    ALU.mult, ALU.add).then_inc(mix_ready, 1)
            mask = cols[:, C_MASK:C_MASK + PAIRS]
            dve.wait_ge(l1_turned, 1)
            nc.vector.tensor_tensor(l1_diag[:], mask.rearrange("p (g a) -> p g a", a=1).broadcast_to([P, PAIRS, HID]),
                                    p_l1w[:, 0:HID].rearrange("p (a h) -> p a h", a=1).broadcast_to([P, PAIRS, HID]),
                                    ALU.mult).then_inc(l1_ready, 1)
            nc.vector.tensor_scalar(l2_diag[:], mask, cols[:, C_L2W:C_L2W + 1], None, ALU.mult).then_inc(l2_ready, 1)

            def turn(slot, first, blocks, t):
                return nc.vector.transpose(
                    turned[t][:, 0:blocks].rearrange("p b t r -> p t b r"),
                    raw[slot][:, :, first * Q:(first + blocks) * Q].rearrange("p t (b f) -> p t b f", f=Q))

            def turn_unit(step, u):
                dve.wait_ge(loaded[u], step * 16 + 16)
                for half in range(2):
                    h = 2 * u + half
                    dve.wait_ge(t_free, step * (2 * STEP_UNITS) + (h + 1))
                    turn(u, half * HALF, HALF, h % T_SLOTS).then_inc(halves_turned, 1)

            with dve.Fori(0, STEPS - 1) as step:
                for u in range(STEP_UNITS):
                    turn_unit(step, u)
            for u in range(STEP_UNITS - 1):
                turn_unit(STEPS - 1, u)
            for i, (first, blocks) in enumerate(TAIL):
                h = 2 * (UNITS - 1) + i
                dve.wait_ge(tail_loaded[i], 16)
                dve.wait_ge(t_free, h + 1)
                turn(STEP_UNITS - 1, first, blocks, h % T_SLOTS).then_inc(halves_turned, 1)
                if i == 0:
                    dve.wait_ge(t_free, T_SLOTS + 2 * (UNITS - 1))
                    dve.wait_ge(mix_ready, 2)
                    nc.vector.tensor_tensor(mixed[0][:], acc[0][:, 0:N], mix[0][:], ALU.mult).then_inc(w_mixed, 1)
            dve.wait_ge(b_summed, 1)
            nc.vector.tensor_tensor(mixed[1][:], acc[1][:, 0:N], mix[1][:], ALU.mult).then_inc(b_mixed, 1)
            dve.wait_ge(x1_sum, 1)
            nc.vector.tensor_scalar(x1[:], p_x1[:, 0:GN], 0.0, 1.0, ALU.max, ALU.min).then_inc(x1_ready, 1)
            dve.wait_ge(x2_sum, 1)
            nc.vector.tensor_scalar(x2[:], p_x2[:, 0:GN], 0.0, 1.0, ALU.max, ALU.min).then_inc(x2_ready, 1)
            dve.wait_ge(y_sum, 1)
            nc.vector.tensor_scalar(y_out[:], p_y[0:PAIRS, 0:GN], cols[0:PAIRS, C_L2B:C_L2B + 1], None, ALU.add).then_inc(y_ready, 1)

        @block.tensor
        def _(pe):
            pe.wait_ge(rows_set, 2)
            pe.wait_ge(rows_in, 16)
            for side in range(SIDES):
                for j in range(NQ):
                    bias = nc.tensor.matmul(acc[side][j * Q:(j + 1) * Q, 0:N], rows[0:1, R_FTB:R_FTB + Q] if j == 0 else zero_row[:],
                                            one_row[:], start=True, stop=False)
                    if side == SIDES - 1:
                        bias.then_inc(t_free, 1)
            nc.tensor.matmul(p_stm[:, 0:N], rows[0:NQ, R_SIGN:R_SIGN + P], rows[0:NQ, R_STM:R_STM + N],
                             start=True, stop=True).then_inc(stm_spread, 1)
            nc.tensor.matmul(p_l1w[:, 0:HID], rows[:, R_L1W:R_L1W + P], rows[:, R_EYE:R_EYE + HID],
                             start=True, stop=True).then_inc(l1_turned, 1)
            nc.tensor.matmul(p_x2[:, 0:GN], rows[0:1, R_L1B:R_L1B + P], one_row[:, 0:GN], start=True, stop=False)

            def multiply(side, s, first, blocks, t, ends=False):
                for b in range(blocks):
                    j = (first + b) % NQ
                    last = nc.tensor.matmul(
                        acc[side][j * Q:(j + 1) * Q, 0:N],
                        w_diag[s][:, first + b].rearrange("p q a o -> p (q a o)"),
                        turned[t][:, b].rearrange("p t r -> p (t r)"),
                        start=False, stop=ends and first + b >= BLOCKS - NQ)
                return last

            def multiply_unit(step, u, ends=False):
                for half in range(2):
                    h = 2 * u + half
                    pe.wait_ge(halves_turned, step * (2 * STEP_UNITS) + (h + 1))
                    last = multiply(u % SIDES, u // SIDES, half * HALF, HALF, h % T_SLOTS, ends)
                    last.then_inc(t_free, 1)

            def multiply_chunk(step, s):
                pe.wait_ge(w_ready, step * (NQ * STEP_CHUNKS) + NQ * (s + 1))
                for side in range(SIDES):
                    multiply_unit(step, s * SIDES + side)

            with pe.Fori(0, STEPS - 1) as step:
                for s in range(STEP_CHUNKS):
                    multiply_chunk(step, s)
            multiply_chunk(STEPS - 1, 0)
            pe.wait_ge(w_ready, NQ * CHUNKS)
            multiply_unit(STEPS - 1, STEP_UNITS - 2, ends=True)

            def add_groups(side):
                for g in range(GROUPS):
                    last = nc.tensor.matmul(p_x1[g * Q:(g + 1) * Q, 0:GN], cols[:, C_SEL:C_SEL + Q],
                                            mixed[side][:].rearrange("p (a g r) -> p g a r", g=GROUPS, r=Q)[:, g], start=side == 0, stop=side == 1)
                return last

            for i, (first, blocks) in enumerate(TAIL):
                h = 2 * (UNITS - 1) + i
                pe.wait_ge(halves_turned, h + 1)
                last = multiply(1, STEP_CHUNKS - 1, first, blocks, h % T_SLOTS, ends=True)
                if i < len(TAIL) - 1:
                    last.then_inc(t_free, 1)
                if i == 1:
                    pe.wait_ge(w_mixed, 1)
                    pe.wait_ge(cols_in, 16)
                    add_groups(0)
            last.then_inc(b_summed, 1)
            pe.wait_ge(b_mixed, 1)
            add_groups(1).then_inc(x1_sum, 1)
            pe.wait_ge(l1_ready, 1)
            pe.wait_ge(x1_ready, 1)
            nc.tensor.matmul(p_x2[:, 0:GN], l1_diag[:].rearrange("p g h -> p (g h)"), x1[:],
                             start=False, stop=True).then_inc(x2_sum, 1)
            pe.wait_ge(l2_ready, 1)
            pe.wait_ge(x2_ready, 1)
            nc.tensor.matmul(p_y[0:PAIRS, 0:GN], l2_diag[:], x2[:], start=True, stop=True).then_inc(y_sum, 1)


def kernel(r_wfts, r_bfts, r_stm, L0_rec_ft_w, L0_rec_ft_b, L0_rec_l1_w, L0_rec_l1_b, L0_rec_l2_w, L0_rec_l2_b):
    import concourse.bacc as bacc
    from concourse.bass_utils import run_bass_kernel_spmd

    nc = bacc.Bacc("TRN2", target_bir_lowering=False, num_devices=1)
    small = [np.asarray(x) for x in (r_stm, L0_rec_ft_b, L0_rec_l1_w, L0_rec_l1_b, L0_rec_l2_w, L0_rec_l2_b)]
    cols, rows = lay_out_parameters(*small)
    arrays = {"wfts": np.asarray(r_wfts), "bfts": np.asarray(r_bfts), "ft_w": np.asarray(L0_rec_ft_w),
              "param_cols": cols, "param_rows": rows}
    args = [nc.dram_tensor(name, a.shape, mybir.dt.from_np(a.dtype), kind="ExternalInput").ap()
            for name, a in arrays.items()]
    out = nc.dram_tensor("out", (ROWS, 1), F32, kind="ExternalOutput").ap()
    evaluate(nc, *args, out)
    return run_bass_kernel_spmd(nc, [arrays], core_ids=[0]).results[0]["out"]
```

```python
from contextlib import ExitStack

import numpy as np

import concourse.bass as bass
from concourse import mybir
from concourse.alu_op_type import AluOpType as ALU

F32 = mybir.dt.float32

P = 128
Q = 32
NQ = P // Q
ROWS, FEATURES = 1024, 5120
TILES = ROWS // P
OUT1 = 4
HID = 2 * OUT1
N = TILES * Q

CHUNKS = 8
UNIT_F = FEATURES // CHUNKS
BLOCKS = UNIT_F // Q
SIDES = 2
HALF_T = TILES // 2
STEP_CHUNKS = 2
STEP_UNITS = STEP_CHUNKS * SIDES
STEPS = CHUNKS // STEP_CHUNKS
UNITS = CHUNKS * SIDES
T_SLOTS = 2
TAIL = ([(2, first, blocks, 0, TILES) for first, blocks in ((0, 10), (10, 5), (15, 5))]
        + [(3, first, 4, 0, TILES) for first in (0, 4, 8)]
        + [(3, 12, 4, tile, 4) for tile in (0, 4)]
        + [(3, 16, 4, tile, tiles) for tile, tiles in ((0, 4), (4, 2), (6, 2))])
ADD_W = 4

GROUPS = NQ
GN = N // GROUPS
PAIRS = GROUPS * NQ

C_SEL, C_MASK, C_OFF, C_REST, C_L2W, C_L2B, C_END = np.cumsum([0, Q, PAIRS, 1, 1, 1, 1]).tolist()
R_SIGN, R_EYE, R_L1W, R_STM, R_FTB, R_L1B, R_END = np.cumsum([0, P, HID, P, N, Q, P]).tolist()


def lay_out_parameters(stm, ft_b, l1_w, l1_b, l2_w, l2_b):
    p = np.arange(P)
    second = p % HID >= OUT1
    cols = np.zeros((P, C_END), np.float32)
    cols[p, C_SEL + p % Q] = 1
    cols[p, C_MASK + p // HID] = 1
    cols[:, C_OFF] = second
    cols[:, C_REST] = ~second
    cols[:, C_L2W] = np.tile(l2_w[0], PAIRS)
    cols[:, C_L2B] = l2_b[0]
    rows = np.zeros((HID, R_END), np.float32)
    rows[p % Q // HID, R_SIGN + p] = np.where(second, -1, 1)
    rows[np.arange(HID), R_EYE + np.arange(HID)] = 1
    rows[:, R_L1W:R_L1W + P] = np.tile(l1_w, (1, PAIRS))
    rows[:NQ, R_STM:R_STM + N] = stm.reshape(TILES, NQ, Q).transpose(1, 0, 2).reshape(NQ, N)
    rows[0, R_FTB:R_FTB + Q] = np.tile(ft_b, Q // OUT1)
    rows[0, R_L1B:R_L1B + P] = np.tile(l1_b, PAIRS)
    return cols, rows


def evaluate(nc, wfts, bfts, ft_w, param_cols, param_rows, out):
    feats = [x.rearrange("(t p) f -> p t f", p=P) for x in (wfts, bfts)]

    with ExitStack() as ctx:
        def sb(name, shape):
            return ctx.enter_context(nc.sbuf_tensor(name, shape, F32))

        def ps(name, shape):
            return ctx.enter_context(nc.psum_tensor(name, shape, F32))

        def sem(name):
            return ctx.enter_context(nc.semaphore(name))

        raw = [sb(f"raw{u}", [P, TILES, UNIT_F]) for u in range(STEP_UNITS)]
        turned = [sb(f"turned{t}", [P, BLOCKS, TILES, Q]) for t in range(T_SLOTS)]
        w_rows = sb("w_rows", [Q, BLOCKS, Q])
        w_cols = sb("w_cols", [Q, BLOCKS, CHUNKS, OUT1])
        w_diag = [sb(f"w_diag{s}", [P, BLOCKS, NQ, 2, OUT1]) for s in range(STEP_CHUNKS)]
        cols = sb("cols", [P, C_END])
        rows = sb("rows", [HID, R_END])
        zero_row = sb("zero_row", [1, Q])
        one_row = sb("one_row", [1, N])
        mix = [sb(f"mix{s}", [P, N]) for s in range(SIDES)]
        l1_diag = sb("l1_diag", [P, PAIRS, HID])
        l2_diag = sb("l2_diag", [P, PAIRS])
        mixed = [sb(f"mixed{s}", [P, N]) for s in range(SIDES)]
        w_sums = sb("w_sums", [P, N])
        x1 = sb("x1", [P, GN])
        x2 = sb("x2", [P, GN])
        y_out = sb("y_out", [PAIRS, GN])

        acc = [ps(f"acc{s}", [P, 512]) for s in range(SIDES)]
        p_stm = ps("p_stm", [P, 512])
        p_l1w = ps("p_l1w", [P, 512])
        p_x1 = ps("p_x1", [P, 512])
        p_x2 = ps("p_x2", [P, 512])
        p_y = ps("p_y", [P, 512])

        loaded = [sem(f"loaded{h}") for h in range(2 * STEP_UNITS)]
        tail_loaded = [sem(f"tail_loaded{i}") for i in range(len(TAIL))]
        w_in = sem("w_in")
        rows_in = sem("rows_in")
        cols_in = sem("cols_in")
        rows_set = sem("rows_set")
        diag_zeroed = sem("diag_zeroed")
        w_turned = sem("w_turned")
        w_ready = sem("w_ready")
        halves_turned = sem("halves_turned")
        t_free = sem("t_free")
        stm_spread = sem("stm_spread")
        l1_turned = sem("l1_turned")
        mix_ready = sem("mix_ready")
        l1_ready = sem("l1_ready")
        l2_ready = sem("l2_ready")
        w_copied = sem("w_copied")
        w_mixed = sem("w_mixed")
        b_summed = sem("b_summed")
        b_mixed = sem("b_mixed")
        x1_sum = sem("x1_sum")
        x1_ready = sem("x1_ready")
        x2_sum = sem("x2_sum")
        x2_ready = sem("x2_ready")
        y_sum = sem("y_sum")
        y_ready = sem("y_ready")
        stored = sem("stored")

        block = ctx.enter_context(nc.Block())

        @block.sync
        def _(sp):
            def load(step, u, first, blocks, tile, tiles):
                side, chunk = u // STEP_CHUNKS, step * STEP_CHUNKS + u % STEP_CHUNKS
                dst = raw[u][:, tile:tile + tiles, first * Q:(first + blocks) * Q]
                src = feats[side][:, tile:tile + tiles, bass.ds(chunk * UNIT_F + first * Q, blocks * Q)]
                return sp.dma_start(dst, src)

            def load_half(step, h):
                load(step, h // 2, 0, BLOCKS, h % 2 * HALF_T, HALF_T).then_inc(loaded[h], 16)

            for h in range(2 * STEP_UNITS):
                load_half(0, h)
                if h == 0:
                    sp.dma_start(w_rows[:].rearrange("p b f -> p (b f)"),
                                 ft_w.rearrange("o (c f) -> c o f", c=CHUNKS)).then_inc(w_in, 16)
                    sp.dma_start(rows[:], param_rows).then_inc(rows_in, 16)
                    sp.dma_start(cols[:], param_cols).then_inc(cols_in, 16)
            with sp.Fori(1, STEPS - 1) as step:
                for h in range(2 * STEP_UNITS):
                    sp.wait_ge(halves_turned, step * (2 * STEP_UNITS) + (h + 1 - 2 * STEP_UNITS))
                    load_half(step, h)
            turned_before = 2 * STEP_UNITS * (STEPS - 2)
            for h in range(2 * STEP_CHUNKS):
                sp.wait_ge(halves_turned, turned_before + h + 1)
                load_half(STEPS - 1, h)
            for i, piece in enumerate(TAIL):
                sp.wait_ge(halves_turned, turned_before + 2 * (piece[0] + 1))
                load(STEPS - 1, *piece).then_inc(tail_loaded[i], 16)
            sp.wait_ge(y_ready, 1)
            sp.dma_start(out.rearrange("(a b r) o -> b a (r o)", a=TILES // GROUPS, r=Q),
                         y_out[:].rearrange("b (a r) -> b a r", r=Q)).then_inc(stored, 16)
            sp.wait_ge(stored, 16)

        @block.gpsimd
        def _(pool):
            nc.gpsimd.memset(zero_row[:], 0.0).then_inc(rows_set, 1)
            nc.gpsimd.memset(one_row[:], 1.0).then_inc(rows_set, 1)
            for s in range(STEP_CHUNKS):
                nc.gpsimd.memset(w_diag[s][:], 0.0).then_inc(diag_zeroed, 1)
            pool.wait_ge(mix_ready, 2)
            pool.wait_ge(w_copied, 1)
            nc.gpsimd.tensor_tensor(mixed[0][:], w_sums[:], mix[0][:], ALU.mult).then_inc(w_mixed, 1)

        @block.scalar
        def _(act):
            def lay_out(chunk, s):
                w = w_cols[:, :, bass.ds(chunk, 1), :].broadcast_to([Q, BLOCKS, 2, OUT1])
                for q in range(NQ):
                    nc.scalar.copy(w_diag[s][q * Q:(q + 1) * Q, :, q], w).then_inc(w_ready, 1)

            act.wait_ge(diag_zeroed, STEP_CHUNKS)
            act.wait_ge(w_turned, 1)
            for s in range(STEP_CHUNKS):
                lay_out(s, s)
            with act.Fori(1, STEPS) as step:
                for s in range(STEP_CHUNKS):
                    act.wait_ge(t_free, step * STEP_UNITS + (T_SLOTS + STEP_CHUNKS + s + 1 - STEP_UNITS))
                    lay_out(step * STEP_CHUNKS + s, s)
            act.wait_ge(t_free, T_SLOTS + UNITS - STEP_CHUNKS)
            nc.scalar.copy(w_sums[:], acc[0][:, 0:N]).then_inc(w_copied, 1)

        @block.vector
        def _(dve):
            dve.wait_ge(w_in, 16)
            nc.vector.transpose(w_cols[:].rearrange("p b c o -> p (b c o)"),
                                w_rows[:].rearrange("p b f -> p (b f)")).then_inc(w_turned, 1)
            dve.wait_ge(cols_in, 16)
            dve.wait_ge(stm_spread, 1)
            nc.vector.tensor_scalar(mix[0][:], p_stm[:, 0:N], cols[:, C_OFF:C_OFF + 1], None,
                                    ALU.add).then_inc(mix_ready, 1)
            nc.vector.tensor_scalar(mix[1][:], p_stm[:, 0:N], -1.0, cols[:, C_REST:C_REST + 1],
                                    ALU.mult, ALU.add).then_inc(mix_ready, 1)
            mask = cols[:, C_MASK:C_MASK + PAIRS]
            whole = [P, PAIRS, HID]
            dve.wait_ge(l1_turned, 1)
            nc.vector.tensor_tensor(l1_diag[:], mask.rearrange("p (g a) -> p g a", a=1).broadcast_to(whole),
                                    p_l1w[:, 0:HID].rearrange("p (a h) -> p a h", a=1).broadcast_to(whole),
                                    ALU.mult).then_inc(l1_ready, 1)
            nc.vector.tensor_scalar(l2_diag[:], mask, cols[:, C_L2W:C_L2W + 1], None,
                                    ALU.mult).then_inc(l2_ready, 1)

            def turn(u, first, blocks, tile, tiles):
                src = raw[u][:, tile:tile + tiles, first * Q:(first + blocks) * Q]
                dst = turned[u % T_SLOTS][:, first:first + blocks, tile:tile + tiles]
                return nc.vector.transpose(dst.rearrange("p b t r -> p t b r"),
                                           src.rearrange("p t (b f) -> p t b f", f=Q))

            def turn_unit(step, u):
                dve.wait_ge(t_free, step * STEP_UNITS + (u + 1))
                for half in range(2):
                    dve.wait_ge(loaded[2 * u + half], step * 16 + 16)
                    turn(u, 0, BLOCKS, half * HALF_T, HALF_T).then_inc(halves_turned, 1)

            with dve.Fori(0, STEPS - 1) as step:
                for u in range(STEP_UNITS):
                    turn_unit(step, u)
            for u in range(STEP_CHUNKS):
                turn_unit(STEPS - 1, u)
            for i, (u, *part) in enumerate(TAIL):
                dve.wait_ge(t_free, STEP_UNITS * (STEPS - 1) + u + 1)
                dve.wait_ge(tail_loaded[i], 16)
                turn(u, *part).then_inc(halves_turned, 1)
            dve.wait_ge(b_summed, 1)
            dve.wait_ge(mix_ready, 2)
            nc.vector.tensor_tensor(mixed[1][:], acc[1][:, 0:N], mix[1][:], ALU.mult).then_inc(b_mixed, 1)
            dve.wait_ge(x1_sum, 1)
            nc.vector.tensor_scalar(x1[:], p_x1[:, 0:GN], 0.0, 1.0, ALU.max, ALU.min).then_inc(x1_ready, 1)
            dve.wait_ge(x2_sum, 1)
            nc.vector.tensor_scalar(x2[:], p_x2[:, 0:GN], 0.0, 1.0, ALU.max, ALU.min).then_inc(x2_ready, 1)
            dve.wait_ge(y_sum, 1)
            nc.vector.tensor_scalar(y_out[:], p_y[0:PAIRS, 0:GN], cols[0:PAIRS, C_L2B:C_L2B + 1], None,
                                    ALU.add).then_inc(y_ready, 1)

        @block.tensor
        def _(pe):
            pe.wait_ge(rows_set, 2)
            pe.wait_ge(rows_in, 16)
            for side in range(SIDES):
                for j in range(NQ):
                    row = rows[0:1, R_FTB:R_FTB + Q] if j == 0 else zero_row[:]
                    bias = nc.tensor.matmul(acc[side][j * Q:(j + 1) * Q, 0:N], row, one_row[:],
                                            start=True, stop=False)
                    if side == SIDES - 1 and j < T_SLOTS:
                        bias.then_inc(t_free, 1)
            nc.tensor.matmul(p_stm[:, 0:N], rows[0:NQ, R_SIGN:R_SIGN + P], rows[0:NQ, R_STM:R_STM + N],
                             start=True, stop=True).then_inc(stm_spread, 1)
            nc.tensor.matmul(p_l1w[:, 0:HID], rows[:, R_L1W:R_L1W + P], rows[:, R_EYE:R_EYE + HID],
                             start=True, stop=True).then_inc(l1_turned, 1)
            nc.tensor.matmul(p_x2[:, 0:GN], rows[0:1, R_L1B:R_L1B + P], one_row[:, 0:GN], start=True, stop=False)

            def multiply(u, first, blocks, tile, tiles, stop=False):
                side, s = u // STEP_CHUNKS, u % STEP_CHUNKS
                for b in range(first, first + blocks):
                    j = b % NQ
                    last = nc.tensor.matmul(
                        acc[side][j * Q:(j + 1) * Q, tile * Q:(tile + tiles) * Q],
                        w_diag[s][:, b].rearrange("p q a o -> p (q a o)"),
                        turned[u % T_SLOTS][:, b, tile:tile + tiles].rearrange("p t r -> p (t r)"),
                        start=False, stop=stop and b >= BLOCKS - NQ)
                return last

            def multiply_unit(step, u, stop=False):
                if u < STEP_CHUNKS:
                    pe.wait_ge(w_ready, step * (NQ * STEP_CHUNKS) + NQ * (u + 1))
                pe.wait_ge(halves_turned, step * (2 * STEP_UNITS) + 2 * (u + 1))
                multiply(u, 0, BLOCKS, 0, TILES, stop).then_inc(t_free, 1)

            with pe.Fori(0, STEPS - 1) as step:
                for u in range(STEP_UNITS):
                    multiply_unit(step, u)
            for u in range(STEP_CHUNKS):
                multiply_unit(STEPS - 1, u, stop=u == STEP_CHUNKS - 1)

            def add_groups(side):
                by_group = mixed[side][:].rearrange("p (a g r) -> p g a r", g=GROUPS, r=Q)
                for g in range(GROUPS):
                    last = nc.tensor.matmul(p_x1[g * Q:(g + 1) * Q, 0:GN], cols[:, C_SEL:C_SEL + Q],
                                            by_group[:, g], start=side == 0, stop=side == SIDES - 1)
                return last

            for i, piece in enumerate(TAIL):
                if i == ADD_W:
                    pe.wait_ge(w_mixed, 1)
                    pe.wait_ge(cols_in, 16)
                    add_groups(0)
                pe.wait_ge(halves_turned, 2 * (UNITS - STEP_CHUNKS) + i + 1)
                last = multiply(*piece, stop=i == len(TAIL) - 1)
            last.then_inc(b_summed, 1)
            pe.wait_ge(b_mixed, 1)
            add_groups(1).then_inc(x1_sum, 1)
            pe.wait_ge(l1_ready, 1)
            pe.wait_ge(x1_ready, 1)
            nc.tensor.matmul(p_x2[:, 0:GN], l1_diag[:].rearrange("p g h -> p (g h)"), x1[:],
                             start=False, stop=True).then_inc(x2_sum, 1)
            pe.wait_ge(l2_ready, 1)
            pe.wait_ge(x2_ready, 1)
            nc.tensor.matmul(p_y[0:PAIRS, 0:GN], l2_diag[:], x2[:], start=True, stop=True).then_inc(y_sum, 1)


def kernel(r_wfts, r_bfts, r_stm, L0_rec_ft_w, L0_rec_ft_b, L0_rec_l1_w, L0_rec_l1_b, L0_rec_l2_w, L0_rec_l2_b):
    import concourse.bacc as bacc
    from concourse.bass_utils import run_bass_kernel_spmd

    nc = bacc.Bacc("TRN2", target_bir_lowering=False, num_devices=1)
    small = [np.asarray(x) for x in (r_stm, L0_rec_ft_b, L0_rec_l1_w, L0_rec_l1_b, L0_rec_l2_w, L0_rec_l2_b)]
    cols, rows = lay_out_parameters(*small)
    arrays = {"wfts": np.asarray(r_wfts), "bfts": np.asarray(r_bfts), "ft_w": np.asarray(L0_rec_ft_w),
              "param_cols": cols, "param_rows": rows}
    args = [nc.dram_tensor(name, a.shape, mybir.dt.from_np(a.dtype), kind="ExternalInput").ap()
            for name, a in arrays.items()]
    out = nc.dram_tensor("out", (ROWS, 1), F32, kind="ExternalOutput").ap()
    evaluate(nc, *args, out)
    return run_bass_kernel_spmd(nc, [arrays], core_ids=[0]).results[0]["out"]
```
